# Optimizing a Trainium2 kernel written in Bass

```python
import numpy as np
import jax
import jax.numpy as jnp

def _softmax(x, axis=-1):
    return jax.nn.softmax(x, axis=axis)

def _gelu(x):
    return jax.nn.gelu(x, approximate=True)

def _silu(x):
    return jax.nn.silu(x)

def _sigmoid(x):
    return jax.nn.sigmoid(x)

def _layernorm(x, axis=-1, eps=1e-05):
    m = jnp.mean(x, axis=axis, keepdims=True)
    v = jnp.var(x, axis=axis, keepdims=True)
    return (x - m) / jnp.sqrt(v + eps)

def _scatter_add(tgt, idx, src, axis=0):
    return tgt.at[idx].add(src)

def _segment_sum(src, seg, n):
    return jax.ops.segment_sum(src, seg, n)
kernel_name = 'mk_gnn_resnorm_d4_gnn_r32_2b060f'

def setup_inputs(seed: int=0):
    np.random.seed(seed)
    _w = jnp.asarray

    def _rec_inputs():
        import jax
        import jax.numpy as jnp
        _gk = jax.random.key(seed)
        x = -0.0005121 + 1.001 * jax.random.normal(jax.random.fold_in(_gk, 1), (50000, 64), jnp.float32)
        src = jax.random.randint(jax.random.fold_in(_gk, 2), (50000,), 0, 50000, jnp.int32)
        dst = jnp.minimum((50000 * jax.random.uniform(jax.random.fold_in(_gk, 3), (50000,)) ** 2.0).astype(jnp.int32), 49999)
        _o = jnp.argsort(dst, stable=True)
        src = src[_o]
        dst = dst[_o]
        edge_attr_64 = jax.random.uniform(jax.random.fold_in(_gk, 12), (50000, 64), jnp.float32, 0.0, 1)
        edge_type_2 = jax.random.randint(jax.random.fold_in(_gk, 14), (50000,), 0, 2, jnp.int32)
        edge_weight = jax.random.uniform(jax.random.fold_in(_gk, 15), (50000,), jnp.float32, 0.0, 4.99999)
        return (x, src, dst, edge_attr_64, edge_type_2, edge_weight)
    x, src, dst, edge_attr_64, edge_type_2, edge_weight = _rec_inputs()

    def _L0_gnn_setup():
        import jax, jax.numpy as jnp
        import numpy as np
        N = 50000
        E = 25000
        DIM = 64
        H = 2
        HID = 128
        NG = 64
        RC = 5.0
        LOG2 = float(np.log(2.0))

        def ssp(v):
            return jax.nn.softplus(v) - LOG2

        def cosine_cutoff(r):
            return 0.5 * (jnp.cos(jnp.pi * r / RC) + 1.0) * (r < RC)
        key = jax.random.key(seed)
        ks = jax.random.split(key, 16)
        x = jax.random.normal(ks[0], (N, DIM), jnp.float32)
        gs = jax.random.uniform(ks[1], (E, NG), jnp.float32)
        rij = jax.random.uniform(ks[2], (E,), jnp.float32) * RC
        src = jax.random.randint(ks[3], (E,), 0, N)
        dst = jax.random.randint(ks[4], (E,), 0, N)

        def w(k, shape, fan_in):
            return jax.random.normal(k, shape, jnp.float32) * (1.0 / np.sqrt(fan_in))
        return {'x': x, 'gs': gs, 'rij': rij, 'src': src, 'dst': dst, 'fc_w': w(ks[5], (DIM, H * DIM), DIM), 'attn_l': w(ks[6], (H, DIM), DIM), 'attn_r': w(ks[7], (H, DIM), DIM), 'filt_w1': w(ks[8], (NG, HID), NG), 'filt_b1': jnp.zeros((HID,), jnp.float32), 'filt_w2': w(ks[9], (HID, H * DIM), HID), 'filt_b2': jnp.zeros((H * DIM,), jnp.float32), 'mlp_w1': w(ks[10], (H * DIM, DIM), H * DIM), 'mlp_b1': jnp.zeros((DIM,), jnp.float32), 'mlp_w2': w(ks[11], (DIM, DIM), DIM), 'mlp_b2': jnp.zeros((DIM,), jnp.float32)}
    _L0_gnn_all = _L0_gnn_setup()
    _L0_gnn_in = {k: v for k, v in _L0_gnn_all.items() if k in ('fc_w', 'attn_l', 'attn_r', 'filt_w1', 'filt_b1', 'filt_w2', 'filt_b2', 'mlp_w1', 'mlp_b1', 'mlp_w2', 'mlp_b2')}
    del _L0_gnn_all

    def _L1_gnn_setup():
        import jax, jax.numpy as jnp
        import numpy as np
        N_NODES = 50000
        N_EDGES = 50000
        IN_FEAT = 64
        OUT_FEAT = 64
        NEG_SLOPE = 0.01
        key = jax.random.key(seed)
        k1, k2, k3, k4, k5 = jax.random.split(key, 5)
        feat = jax.random.normal(k1, (N_NODES, IN_FEAT), dtype=jnp.float32)
        W = jax.random.normal(k2, (IN_FEAT, OUT_FEAT), dtype=jnp.float32) * (1.0 / np.sqrt(IN_FEAT))
        b = jax.random.normal(k3, (OUT_FEAT,), dtype=jnp.float32) * 0.01
        src = jax.random.randint(k4, (N_EDGES,), 0, N_NODES, dtype=jnp.int64 if jax.config.jax_enable_x64 else jnp.int32)
        dst = jax.random.randint(k5, (N_EDGES,), 0, N_NODES, dtype=jnp.int64 if jax.config.jax_enable_x64 else jnp.int32)
        return {'feat': feat, 'W': W, 'b': b, 'src': src, 'dst': dst}
    _L1_gnn_all = _L1_gnn_setup()
    _L1_gnn_in = {k: v for k, v in _L1_gnn_all.items() if k in ('W', 'b')}
    del _L1_gnn_all

    def _L2_gnn_setup():
        import jax, jax.numpy as jnp
        import numpy as np

        def gin_layer(x, src, dst, ew, w1, b1, w2, b2):
            msg = x[src] * ew[:, None]
            agg = jax.ops.segment_sum(msg, dst, num_segments=x.shape[0])
            h = agg + x
            h = jax.nn.relu(h @ w1 + b1)
            return h @ w2 + b2
        key = jax.random.key(seed)
        ks = jax.random.split(key, 16)
        N, E, D = (3125, 31250, 64)
        x = jax.random.normal(ks[0], (N, D), dtype=jnp.float32)
        edge_index = jax.random.randint(ks[1], (2, E), 0, N)
        edge_weight = jax.random.uniform(ks[2], (E,), dtype=jnp.float32)

        def lin(k, fi, fo):
            return jax.random.normal(k, (fi, fo), dtype=jnp.float32) * (1.0 / np.sqrt(fi))
        return {'x': x, 'edge_index': edge_index, 'edge_weight': edge_weight, 'w11': lin(ks[3], 64, 64), 'b11': jnp.zeros(64, jnp.float32), 'w12': lin(ks[4], 64, 64), 'b12': jnp.zeros(64, jnp.float32), 'w21': lin(ks[5], 64, 128), 'b21': jnp.zeros(128, jnp.float32), 'w22': lin(ks[6], 128, 64), 'b22': jnp.zeros(64, jnp.float32), 'w31': lin(ks[7], 64, 64), 'b31': jnp.zeros(64, jnp.float32), 'w32': lin(ks[8], 64, 64), 'b32': jnp.zeros(64, jnp.float32)}
    _L2_gnn_all = _L2_gnn_setup()
    _L2_gnn_in = {k: v for k, v in _L2_gnn_all.items() if k in ('w11', 'b11', 'w12', 'b12', 'w21', 'b21', 'w22', 'b22', 'w31', 'b31', 'w32', 'b32')}
    del _L2_gnn_all

    def _L3_gnn_setup():
        import jax, jax.numpy as jnp
        import numpy as np
        N_NODES = 3125
        N_EDGES = 31250
        DIM = 64

        def rel_graph_conv(x, src, dst, etype, W, Ws, b, act):
            h = jnp.einsum('nd,rdo->rno', x, W)
            m = jnp.where((etype == 0)[:, None], h[0][src], h[1][src])
            agg = jax.ops.segment_sum(m, dst, num_segments=x.shape[0])
            out = agg + x @ Ws + b
            return act(out) if act is not None else out
        key = jax.random.key(seed)
        ks = jax.random.split(key, 16)
        scale = 1.0 / np.sqrt(DIM)
        inp = {'features': jax.random.normal(ks[0], (N_NODES, DIM), dtype=jnp.float32), 'src': jax.random.randint(ks[1], (N_EDGES,), 0, N_NODES, dtype=jnp.int32), 'dst': jax.random.randint(ks[2], (N_EDGES,), 0, N_NODES, dtype=jnp.int32), 'etype': jax.random.randint(ks[3], (N_EDGES,), 0, 2, dtype=jnp.int32)}
        for i in range(3):
            inp[f'W{i}'] = jax.random.normal(ks[4 + 3 * i], (2, DIM, DIM), dtype=jnp.float32) * scale
            inp[f'Ws{i}'] = jax.random.normal(ks[5 + 3 * i], (DIM, DIM), dtype=jnp.float32) * scale
            inp[f'b{i}'] = jnp.zeros((DIM,), dtype=jnp.float32)
        return inp
    _L3_gnn_all = _L3_gnn_setup()
    _L3_gnn_in = {k: v for k, v in _L3_gnn_all.items() if k in ('W0', 'Ws0', 'b0', 'W1', 'Ws1', 'b1', 'W2', 'Ws2', 'b2')}
    del _L3_gnn_all
    return {'x': x, 'src': src, 'dst': dst, 'edge_attr_64': edge_attr_64, 'edge_type_2': edge_type_2, 'edge_weight': edge_weight, 'L0_gnn_fc_w': _L0_gnn_in['fc_w'], 'L0_gnn_attn_l': _L0_gnn_in['attn_l'], 'L0_gnn_attn_r': _L0_gnn_in['attn_r'], 'L0_gnn_filt_w1': _L0_gnn_in['filt_w1'], 'L0_gnn_filt_b1': _L0_gnn_in['filt_b1'], 'L0_gnn_filt_w2': _L0_gnn_in['filt_w2'], 'L0_gnn_filt_b2': _L0_gnn_in['filt_b2'], 'L0_gnn_mlp_w1': _L0_gnn_in['mlp_w1'], 'L0_gnn_mlp_b1': _L0_gnn_in['mlp_b1'], 'L0_gnn_mlp_w2': _L0_gnn_in['mlp_w2'], 'L0_gnn_mlp_b2': _L0_gnn_in['mlp_b2'], 'L1_gnn_W': _L1_gnn_in['W'], 'L1_gnn_b': _L1_gnn_in['b'], 'L2_gnn_w11': _L2_gnn_in['w11'], 'L2_gnn_b11': _L2_gnn_in['b11'], 'L2_gnn_w12': _L2_gnn_in['w12'], 'L2_gnn_b12': _L2_gnn_in['b12'], 'L2_gnn_w21': _L2_gnn_in['w21'], 'L2_gnn_b21': _L2_gnn_in['b21'], 'L2_gnn_w22': _L2_gnn_in['w22'], 'L2_gnn_b22': _L2_gnn_in['b22'], 'L2_gnn_w31': _L2_gnn_in['w31'], 'L2_gnn_b31': _L2_gnn_in['b31'], 'L2_gnn_w32': _L2_gnn_in['w32'], 'L2_gnn_b32': _L2_gnn_in['b32'], 'L3_gnn_W0': _L3_gnn_in['W0'], 'L3_gnn_Ws0': _L3_gnn_in['Ws0'], 'L3_gnn_b0': _L3_gnn_in['b0'], 'L3_gnn_W1': _L3_gnn_in['W1'], 'L3_gnn_Ws1': _L3_gnn_in['Ws1'], 'L3_gnn_b1': _L3_gnn_in['b1'], 'L3_gnn_W2': _L3_gnn_in['W2'], 'L3_gnn_Ws2': _L3_gnn_in['Ws2'], 'L3_gnn_b2': _L3_gnn_in['b2']}

def reference(x, src, dst, edge_attr_64, edge_type_2, edge_weight, L0_gnn_fc_w, L0_gnn_attn_l, L0_gnn_attn_r, L0_gnn_filt_w1, L0_gnn_filt_b1, L0_gnn_filt_w2, L0_gnn_filt_b2, L0_gnn_mlp_w1, L0_gnn_mlp_b1, L0_gnn_mlp_w2, L0_gnn_mlp_b2, L1_gnn_W, L1_gnn_b, L2_gnn_w11, L2_gnn_b11, L2_gnn_w12, L2_gnn_b12, L2_gnn_w21, L2_gnn_b21, L2_gnn_w22, L2_gnn_b22, L2_gnn_w31, L2_gnn_b31, L2_gnn_w32, L2_gnn_b32, L3_gnn_W0, L3_gnn_Ws0, L3_gnn_b0, L3_gnn_W1, L3_gnn_Ws1, L3_gnn_b1, L3_gnn_W2, L3_gnn_Ws2, L3_gnn_b2):
    import jax
    import jax.numpy as jnp

    def _L0_gnn_ref(x, gs, rij, src, dst, fc_w, attn_l, attn_r, filt_w1, filt_b1, filt_w2, filt_b2, mlp_w1, mlp_b1, mlp_w2, mlp_b2):
        import jax, jax.numpy as jnp
        import numpy as np
        N = 50000
        E = 25000
        DIM = 64
        H = 2
        HID = 128
        NG = 64
        RC = 5.0
        LOG2 = float(np.log(2.0))

        def ssp(v):
            return jax.nn.softplus(v) - LOG2

        def cosine_cutoff(r):
            return 0.5 * (jnp.cos(jnp.pi * r / RC) + 1.0) * (r < RC)
        n = x.shape[0]
        feat = (x @ fc_w).reshape(n, H, DIM)
        el = jnp.sum(feat * attn_l, axis=-1)
        er = jnp.sum(feat * attn_r, axis=-1)
        e = jax.nn.leaky_relu(el[src] + er[dst], 0.2)
        m = jax.ops.segment_max(e, dst, num_segments=n)
        m = jnp.where(jnp.isfinite(m), m, 0.0)
        ex = jnp.exp(e - m[dst])
        den = jax.ops.segment_sum(ex, dst, num_segments=n)
        alpha = ex / jnp.maximum(den[dst], 1e-16)
        filt = (ssp(gs @ filt_w1 + filt_b1) @ filt_w2 + filt_b2).reshape(-1, H, DIM)
        coef = alpha * cosine_cutoff(rij)[:, None]
        msg = feat[src] * filt * coef[:, :, None]
        agg = jax.ops.segment_sum(msg, dst, num_segments=n)
        res = ssp(agg).reshape(n, H * DIM)
        res = ssp(res @ mlp_w1 + mlp_b1) @ mlp_w2 + mlp_b2
        return res

    def _L1_gnn_ref(feat, W, b, src, dst):
        import jax, jax.numpy as jnp
        import numpy as np
        N_NODES = 50000
        N_EDGES = 50000
        IN_FEAT = 64
        OUT_FEAT = 64
        NEG_SLOPE = 0.01
        e = feat[dst] - feat[src]
        h = jax.nn.leaky_relu(e @ W + b, NEG_SLOPE)
        out = jax.ops.segment_max(h, dst, num_segments=feat.shape[0])
        return jnp.where(jnp.isneginf(out), jnp.zeros_like(out), out)

    def _L2_gnn_ref(x, edge_index, edge_weight, w11, b11, w12, b12, w21, b21, w22, b22, w31, b31, w32, b32):
        import jax, jax.numpy as jnp
        import numpy as np

        def gin_layer(x, src, dst, ew, w1, b1, w2, b2):
            msg = x[src] * ew[:, None]
            agg = jax.ops.segment_sum(msg, dst, num_segments=x.shape[0])
            h = agg + x
            h = jax.nn.relu(h @ w1 + b1)
            return h @ w2 + b2
        src, dst = (edge_index[0], edge_index[1])
        h = gin_layer(x, src, dst, edge_weight, w11, b11, w12, b12)
        h = jax.nn.relu(h)
        h = gin_layer(h, src, dst, edge_weight, w21, b21, w22, b22)
        h = jax.nn.relu(h)
        h = gin_layer(h, src, dst, edge_weight, w31, b31, w32, b32)
        return h

    def _L3_gnn_ref(features, src, dst, etype, W0, Ws0, b0, W1, Ws1, b1, W2, Ws2, b2):
        import jax, jax.numpy as jnp
        import numpy as np
        N_NODES = 3125
        N_EDGES = 31250
        DIM = 64

        def rel_graph_conv(x, src, dst, etype, W, Ws, b, act):
            h = jnp.einsum('nd,rdo->rno', x, W)
            m = jnp.where((etype == 0)[:, None], h[0][src], h[1][src])
            agg = jax.ops.segment_sum(m, dst, num_segments=x.shape[0])
            out = agg + x @ Ws + b
            return act(out) if act is not None else out
        h = rel_graph_conv(features, src, dst, etype, W0, Ws0, b0, jax.nn.relu)
        h = rel_graph_conv(h, src, dst, etype, W1, Ws1, b1, jax.nn.relu)
        h = rel_graph_conv(h, src, dst, etype, W2, Ws2, b2, None)
        return h
    edge_index = jnp.stack([src, dst])
    x = _layernorm(x + _L0_gnn_ref(x, edge_attr_64, edge_weight, src, dst, L0_gnn_fc_w, L0_gnn_attn_l, L0_gnn_attn_r, L0_gnn_filt_w1, L0_gnn_filt_b1, L0_gnn_filt_w2, L0_gnn_filt_b2, L0_gnn_mlp_w1, L0_gnn_mlp_b1, L0_gnn_mlp_w2, L0_gnn_mlp_b2), axis=-1)
    x = _layernorm(x + _L1_gnn_ref(x, L1_gnn_W, L1_gnn_b, src, dst), axis=-1)
    x = _layernorm(x + _L2_gnn_ref(x, edge_index, edge_weight, L2_gnn_w11, L2_gnn_b11, L2_gnn_w12, L2_gnn_b12, L2_gnn_w21, L2_gnn_b21, L2_gnn_w22, L2_gnn_b22, L2_gnn_w31, L2_gnn_b31, L2_gnn_w32, L2_gnn_b32), axis=-1)
    x = _layernorm(x + _L3_gnn_ref(x, src, dst, edge_type_2, L3_gnn_W0, L3_gnn_Ws0, L3_gnn_b0, L3_gnn_W1, L3_gnn_Ws1, L3_gnn_b1, L3_gnn_W2, L3_gnn_Ws2, L3_gnn_b2), axis=-1)
    return x

_drawn_inputs = setup_inputs


def setup_inputs(seed=0):
    import zlib

    import numpy as np

    out = dict(_drawn_inputs(seed))
    spreads = {'L0_gnn_filt_b1': (0.0, 0.8),
     'L0_gnn_filt_b2': (0.0, 2.0),
     'L0_gnn_mlp_b1': (0.0, 0.1),
     'L0_gnn_mlp_b2': (0.0, 0.1),
     'L2_gnn_b11': (0.0, 0.278),
     'L2_gnn_b12': (0.0, 0.1),
     'L2_gnn_b21': (0.0, 0.1),
     'L2_gnn_b22': (0.0, 0.1),
     'L2_gnn_b31': (0.0, 0.1),
     'L2_gnn_b32': (0.0, 0.1),
     'L3_gnn_b0': (0.0, 0.1),
     'L3_gnn_b1': (0.0, 0.1),
     'L3_gnn_b2': (0.0, 0.1)}
    factors = {'edge_attr_64': 5.382,
     'L0_gnn_fc_w': 2.775,
     'L0_gnn_attn_l': 8.0,
     'L0_gnn_attn_r': 31.096,
     'L0_gnn_filt_w1': 2.897,
     'L0_gnn_filt_w2': 2.987,
     'L0_gnn_mlp_w1': 2.869,
     'L1_gnn_b': 28.555}
    for name, (base, spread) in spreads.items():
        noise = np.random.default_rng([zlib.crc32(name.encode()), seed]).standard_normal(out[name].shape)
        drawn = base * np.exp(spread * noise) if base else spread * noise
        out[name] = jnp.asarray(drawn.astype(out[name].dtype))
    for name, factor in factors.items():
        out[name] = (out[name] * factor).astype(out[name].dtype)
    return out
```

```python
from contextlib import ExitStack

import concourse.bass as bass
from concourse import mybir

ALU = mybir.AluOpType
ACT = mybir.ActivationFunctionType
F32 = mybir.dt.float32
I32 = mybir.dt.int32
U32 = mybir.dt.uint32
AX = mybir.AxisListType.X

P = 128
D = 64
HD = 2 * D
GROUP = 2 * P
CHUNK = 4
SLOTS = 7
ROW0 = HD + 4
MW = D + 1
LOG2 = 0.6931471805599453
CUTOFF = 5.0
BIG = 1e30
EPS = 1e-5


def sizes(n_nodes, n_edges):
    ring = 2 * CHUNK * SLOTS * P
    tiles = (n_edges // ring + 1) * 2 * CHUNK * SLOTS
    groups = -(-n_nodes // GROUP)
    return tiles, groups


def build(nc, a, out):
    NP = a["x_rows"].shape[0]
    NG = NP // GROUP
    T = a["src_tiles"].shape[1]
    EP = T * P
    NCH = T // CHUNK
    LOOPS = NCH // SLOTS
    Q = T // 4
    SC = EP // 16

    ctx = ExitStack()
    with ctx:
        def sb(name, shape, dt=F32):
            return ctx.enter_context(nc.sbuf_tensor(name, shape, dt))

        def dram(name, shape):
            return nc.dram_tensor(name, shape, F32, kind="Internal").ap()

        table0 = dram("table0", (NP, ROW0))
        er_table = dram("er_table", (NP, 2))
        spill = dram("spill", (P, T * D))
        flat_e = dram("flat_e", (2, EP))
        flat_f = dram("flat_f", (2, EP))
        flat_m = dram("flat_m", (2, EP))
        same_prev = dram("same_prev", (1, EP))
        same_next = dram("same_next", (1, EP))
        head0 = dram("head0", (NP, D))
        x1 = dram("x1", (NP, D))
        x2 = dram("x2", (NP, D))
        x3 = dram("x3", (NP, D))
        y_table = dram("y_table", (NP, D))
        yb_rows = dram("yb_rows", (NP, D))
        gin_a = dram("gin_a", (NP, D))
        gin_b = dram("gin_b", (NP, D))
        rel_a = dram("rel_a", (NP, HD))
        rel_b = dram("rel_b", (NP, HD))
        self_a = dram("self_a", (NP, D))
        self_b = dram("self_b", (NP, D))

        msg = sb("msg", [P, (T + 2) * MW])
        ring = sb("ring", [P, SLOTS * CHUNK * ROW0])
        er_ring = sb("er_ring", [P, SLOTS * CHUNK * 2])
        dst_f = sb("dst_f", [P, T + 2])
        last_w = sb("last_w", [P, T + 2])
        ew = sb("ew", [P, T + 2])
        cut = sb("cut", [P, T])
        exw = sb("exw", [P, T + 2, 2])
        src_u = sb("src_u", [P, T], U32)
        dst_u = sb("dst_u", [P, T], U32)
        rel_u = sb("rel_u", [P, T], U32)
        idx_now = sb("idx_now", [P, 2, CHUNK * SLOTS], U32)
        dst_now = sb("dst_now", [P, 2, CHUNK * SLOTS], U32)
        gbase = sb("gbase", [P, NG + 1])
        lane = sb("lane", [P, GROUP])
        node_ids = sb("node_ids", [P, GROUP])
        ident = sb("ident", [P, P])
        sel = sb("sel", [P, 2, GROUP])
        runs = sb("runs", [1, NG * 4], I32)
        wts = sb("wts", [P, 24 * D])
        bias = sb("bias", [P, 16])
        rows = sb("rows", [1, 1024])
        work = sb("work", [P, 7 * 512])
        small = sb("small", [P, 64])
        sloop = sb("sloop", [P, 16])

        psum = [ctx.enter_context(nc.psum_tensor(f"bank{i}", [P, 512], F32)) for i in range(8)]

        sems = {f"gathered_s{q}": ctx.enter_context(nc.semaphore(f"gathered_s{q}")) for q in range(SLOTS)}
        gathered_before = [0]
        SEM_NAMES = ("loaded loaded2 made turned "
                     "idx_ready idx_read slot_free slot_used placed msgs_ready sel_ready "
                     "sel_free agg_ready agg_taken node_in node_in_free evac vsum turned_v vt_ready hid_ready "
                     "act_ready act2_ready res_ready stat_ready rstd_ready xn_ready stored out_ready out_free "
                     "soft_abs soft_exp soft_ln soft_done soft2_abs soft2_exp soft2_ln soft2_done step chunk_in "
                     "hid_free filt_ready filt_free scan_done back_ready er_here head_copied rows_ready xt_ready "
                     "tab_ready tab_copied tab_copied2 tab_stored ln_step held written").split()
        for s in SEM_NAMES:
            sems[s] = ctx.enter_context(nc.semaphore(s))
        first_sem = sems[SEM_NAMES[0]].num
        S = sems

        def hold(eng, sem, value):
            eng.wait_ge(sem, value)
            eng.sem_inc(S["held"], 1)

        def new_phase():
            nc.all_engine_barrier(sems_to_clear=range(first_sem, first_sem + len(SEM_NAMES)))

        def from_one(eng, *names):
            for name in names:
                eng.sem_inc(S[name], 1)

        at = {}
        col = 0
        for name, width in (("fcx", ROW0), ("filt_w1", HD), ("filt_w2", HD), ("mlp_w1", D), ("mlp_w2", D),
                            ("W1W1", HD), ("w11", D), ("w12", D), ("w21", HD), ("w22", D), ("w31", D),
                            ("w32", D), ("R0", 3 * D), ("R1", 3 * D)):
            at[name] = (col, width)
            col += width
        assert col <= 24 * D
        R2_AT = 0

        def w(name, k):
            c, n = at[name]
            return wts[0:k, c:c + n]

        rat = {}
        col = 0
        for name, width in (("filt_b2", HD), ("mlp_b2", D), ("yb", HD), ("b12", D), ("b22", D), ("b32", D),
                            ("rb0", 3 * D), ("rb1", 3 * D)):
            rat[name] = (col, width)
            col += width
        assert col <= 1024
        rb2 = sb("rb2", [1, 3 * D])
        R2 = sb("R2", [D, 3 * D])
        zrow = sb("zrow", [1, 512])
        orow = sb("orow", [1, P])

        def row(name):
            c, n = rat[name]
            return rows[0:1, c:c + n]

        B1, MB1, B11, B21, B31, EPSC, ONE, HALFPI, NLOG2 = range(9)

        with nc.Block() as block:
            raw_i = work[:, 0:T].bitcast(I32)
            raw_j = work[:, 512:512 + T].bitcast(I32)
            raw_k = work[:, 1024:1024 + T].bitcast(I32)
            prev_f = work[:, 1536:1536 + T]
            next_f = work[:, 2048:2048 + T]
            flat_f32 = work[:, 2560:2560 + T]
            first_f = small[0:Q, 0:4]
            last_f = small[0:Q, 4:8]
            gb0 = ring[0:Q, 0:NG]
            cmp = ring[0:Q, 256:256 + NG]
            cmp2 = ring[0:Q, 512:512 + NG]
            attn = ring[0:D, 2048:2048 + 2 * HD]
            prod = ring[0:D, 2304:2304 + 2 * HD]
            r = [ring[0:1, 2048 + 256 * i:2048 + 256 * i + NG] for i in range(6)]
            ints = er_ring

            loads = [
                (src_u[:, :].bitcast(I32), a["src_tiles"]), (raw_i, a["dst_tiles"]), (raw_j, a["type_tiles"]),
                (ew[:, 0:T], a["ew_tiles"]), (ident[:, :], a["identity"]), (gbase[:, 0:NG], a["group_base"]),
                (lane[:, :], a["lane"]), (w("fcx", D)[:, 0:HD], a["fc_w"]), (w("filt_w1", D), a["filt_w1"]),
                (w("filt_w2", P), a["filt_w2"]), (w("mlp_w1", P), a["mlp_w1"]), (w("mlp_w2", D), a["mlp_w2"]),
                (w("W1W1", D)[:, 0:D], a["L1_W"]), (w("W1W1", D)[:, D:HD], a["L1_W"]),
                (w("w11", D), a["w11"]), (w("w12", D), a["w12"]), (w("w21", D), a["w21"]), (w("w22", P), a["w22"]),
                (w("w31", D), a["w31"]), (w("w32", D), a["w32"]),
                (w("R0", D), a["R0"]), (w("R1", D), a["R1"]), (R2[:, :], a["R2"]),
                (bias[:, B1:B1 + 1], a["filt_b1"]), (bias[0:D, MB1:MB1 + 1], a["mlp_b1"]),
                (bias[0:D, B11:B11 + 1], a["b11"]), (bias[:, B21:B21 + 1], a["b21"]),
                (bias[0:D, B31:B31 + 1], a["b31"]),
                (row("filt_b2"), a["filt_b2"]), (row("mlp_b2"), a["mlp_b2"]), (row("yb")[:, D:HD], a["L1_b"]),
                (row("b12"), a["b12"]), (row("b22"), a["b22"]), (row("b32"), a["b32"]),
                (row("rb0")[:, 2 * D:3 * D], a["b0"]), (row("rb1")[:, 2 * D:3 * D], a["b1"]),
                (rb2[:, 2 * D:3 * D], a["b2"]),
                (attn[:, 0:HD], a["attn_l"].partition_broadcast(D)),
                (attn[:, HD:2 * HD], a["attn_r"].partition_broadcast(D)),
            ]
            tile_ends = small[0:Q, 32:40].bitcast(I32)

            @block.sync
            def _(sp):
                for dst, src in loads:
                    sp.dma_start(dst, src).then_inc(S["loaded"], 16)
                sp.dma_start(tile_ends, a["tile_ends"]).then_inc(S["loaded"], 16)
                sp.dma_start(raw_k, a["dst_flat"]).then_inc(S["loaded"], 16)
                sp.wait_ge(S["made"], 1)
                sp.dma_start(raw_k, a["prev_flat"]).then_inc(S["loaded2"], 16)
                sp.wait_ge(S["made"], 2)
                sp.dma_start(raw_k, a["next_flat"]).then_inc(S["loaded2"], 16)
                sp.wait_ge(S["made"], 3)
                sp.dma_start(raw_k, a["next_tiles"]).then_inc(S["loaded2"], 16)
                sp.wait_ge(S["made"], 4)
                sp.dma_start(same_prev.rearrange("o (p j) -> (o p) j", p=P), prev_f).then_inc(S["written"], 16)
                sp.dma_start(same_next.rearrange("o (p j) -> (o p) j", p=P), next_f).then_inc(S["written"], 16)
                sp.wait_ge(S["written"], 32)

            n_loads = len(loads) + 2

            @block.vector
            def _(dve):
                n = [0]

                def then(ins):
                    n[0] += 1
                    ins.then_inc(S["step"], 1)
                    dve.wait_ge(S["step"], n[0])

                v = nc.vector
                v.memset(msg[:, :], 0.0)
                v.memset(dst_f[:, :], float(NP))
                v.memset(ew[:, T:T + 2], 0.0)
                v.memset(last_w[:, :], 0.0)
                v.memset(exw[:, :, :], 0.0)
                v.memset(zrow[:, :], 0.0)
                v.memset(orow[:, :], 1.0)
                v.memset(row("yb")[:, 0:D], 0.0)
                v.memset(row("rb0")[:, 0:2 * D], 0.0)
                v.memset(row("rb1")[:, 0:2 * D], 0.0)
                v.memset(rb2[:, 0:2 * D], 0.0)
                v.memset(bias[:, EPSC:EPSC + 1], EPS)
                v.memset(bias[:, ONE:ONE + 1], 1.0)
                v.memset(bias[:, HALFPI:HALFPI + 1], 1.5707963267948966)
                v.memset(bias[:, NLOG2:NLOG2 + 1], -LOG2)
                then(v.memset(small[:, 8:9], 1.0))
                dve.wait_ge(S["loaded"], 16 * n_loads)
                v.tensor_copy(flat_f32, raw_k).then_inc(S["made"], 1)
                v.tensor_copy(dst_f[:, 0:T], raw_i)
                v.tensor_scalar(ring[:, 0:T], raw_j, 0.0, None, ALU.not_equal)
                then(v.tensor_copy(ring[:, 512:512 + T], src_u[:, :].bitcast(I32)))
                v.tensor_scalar(dst_u[:, :], dst_f[:, 0:T], float(NP - 1), None, ALU.min)
                then(v.scalar_tensor_tensor(rel_u[:, :], ring[:, 512:512 + T], 2.0, ring[:, 0:T], ALU.mult, ALU.add))
                dve.wait_ge(S["loaded2"], 16)
                then(v.tensor_copy(prev_f, raw_k))
                then(v.tensor_tensor(prev_f, prev_f, flat_f32, ALU.not_equal))
                v.tensor_scalar(prev_f, prev_f, BIG, None, ALU.mult).then_inc(S["made"], 1)
                dve.wait_ge(S["loaded2"], 32)
                then(v.tensor_copy(next_f, raw_k))
                then(v.tensor_tensor(next_f, next_f, flat_f32, ALU.not_equal))
                v.tensor_scalar(next_f, next_f, -BIG, None, ALU.mult).then_inc(S["made"], 1)
                dve.wait_ge(S["loaded2"], 48)
                then(v.tensor_copy(ring[:, 0:T], raw_k))
                v.tensor_tensor(last_w[:, 0:T], ring[:, 0:T], dst_f[:, 0:T], ALU.not_equal).then_inc(S["made"], 1)
                dve.wait_ge(S["made"], 4)
                then(v.tensor_scalar(ring[:, 512:512 + T], ew[:, 0:T], CUTOFF, 0.0, ALU.min, ALU.max))
                v.tensor_scalar(ring[:, 1024:1024 + T], ew[:, 0:T], CUTOFF, 0.5, ALU.is_lt, ALU.mult).then_inc(S["made"], 1)
                dve.wait_ge(S["turned"], 1)
                then(v.scalar_tensor_tensor(cut[:, :], ring[:, 1536:1536 + T], 1.0, ring[:, 1024:1024 + T],
                                            ALU.add, ALU.mult))
                for side in range(2):
                    then(v.tensor_tensor(prod[:, side * HD:(side + 1) * HD], w("fcx", D)[:, 0:HD],
                                         attn[:, side * HD:(side + 1) * HD], ALU.mult))
                then(v.tensor_reduce(w("fcx", D)[:, HD:ROW0], prod.rearrange("p (s d) -> p s d", d=D), AX, ALU.add))
                then(v.tensor_copy(small[0:Q, 0:8], tile_ends))
                then(v.tensor_copy(gb0, gbase[0:Q, 0:NG]))
                for b in range(4):
                    if b:
                        dve.wait_ge(S["hid_free"], b + 1)
                    v.tensor_scalar(cmp, gb0, last_f[:, b:b + 1], None, ALU.is_gt)
                    then(v.tensor_scalar(cmp2, gb0, float(GROUP), None, ALU.add))
                    v.tensor_scalar(cmp2, cmp2, first_f[:, b:b + 1], None, ALU.is_gt).then_inc(S["hid_ready"], 1)
                dve.wait_ge(S["hid_free"], 5)
                start_ps, end_ps = psum[0][0:1, 0:NG], psum[1][0:1, 0:NG]
                then(v.tensor_copy(r[0], start_ps))
                then(v.scalar_tensor_tensor(r[1], r[0], 1.0, end_ps, ALU.add, ALU.max))
                then(v.scalar_tensor_tensor(r[2], r[0], -1.0, r[1], ALU.mult, ALU.add))
                then(v.tensor_scalar(r[2], r[2], 1.0, None, ALU.add))
                then(v.tensor_copy(r[3].bitcast(I32), r[2]))
                then(v.tensor_scalar(r[3].bitcast(I32), r[3].bitcast(I32), 1, None, ALU.arith_shift_right))
                then(v.tensor_copy(r[2], r[3].bitcast(I32)))
                then(v.memset(r[4], 0.0))
                then(v.tensor_tensor_scan(r[5], r[2], r[4], 0.0, ALU.add, ALU.add))
                then(v.tensor_tensor(r[4], r[5], r[2], ALU.subtract))
                rv = runs[:, :].rearrange("o (g f) -> o g f", f=4)
                v.memset(runs[:, :], 0)
                then(v.memset(small[0:1, 9:10], 0.0))
                v.tensor_copy(rv[:, :, 0], r[0])
                then(v.scalar_tensor_tensor(r[1], r[2], 2.0, r[0], ALU.mult, ALU.add))
                v.tensor_copy(rv[:, :, 1], r[1])
                then(v.scalar_tensor_tensor(r[3], r[4], 2.0, r[0], ALU.mult, ALU.subtract))
                then(v.tensor_copy(rv[:, :, 2], r[3]))
                dve.wait_ge(S["tab_ready"], 1)
                then(v.tensor_tensor(row("filt_b2"), row("filt_b2"), psum[2][0:1, 0:HD], ALU.add))
                then(v.tensor_tensor(row("mlp_b2"), row("mlp_b2"), psum[3][0:1, 0:D], ALU.add))
                then(v.tensor_tensor(bias[0:D, MB1:MB1 + 1], bias[0:D, MB1:MB1 + 1], psum[4][0:D, 0:1], ALU.add))

            @block.scalar
            def _(act):
                act.wait_ge(S["made"], 5)
                nc.scalar.activation(ring[:, 1536:1536 + T], ring[:, 512:512 + T], ACT.Sin,
                                     bias=bias[:, HALFPI:HALFPI + 1],
                                     scale=-3.141592653589793 / CUTOFF).then_inc(S["turned"], 1)

            @block.tensor
            def _(pe):
                from_one(pe, "hid_free")
                pe.wait_ge(S["loaded"], 16 * n_loads)
                pe.wait_ge(S["step"], 1)
                for b in range(4):
                    pe.wait_ge(S["hid_ready"], b + 1)
                    nc.tensor.matmul(psum[0][0:1, 0:NG], small[0:Q, 8:9], cmp, start=(b == 0), stop=(b == 3))
                    nc.tensor.matmul(psum[1][0:1, 0:NG], small[0:Q, 8:9], cmp2, start=(b == 0),
                                     stop=(b == 3)).then_inc(S["hid_free"], 1)
                nc.tensor.matmul(psum[2][0:1, 0:HD], bias[:, NLOG2:NLOG2 + 1], w("filt_w2", P), start=True, stop=True)
                nc.tensor.matmul(psum[3][0:1, 0:D], bias[0:D, NLOG2:NLOG2 + 1], w("mlp_w2", D), start=True, stop=True)
                nc.tensor.matmul(psum[4][0:D, 0:1], w("mlp_w1", P), bias[:, NLOG2:NLOG2 + 1],
                                 start=True, stop=True).then_inc(S["tab_ready"], 1)
        new_phase()

        def group_rows(table, g, width):
            return table.rearrange("(g p a) d -> p g (a d)", p=P, a=2)[:, bass.ds(g, 1), :].rearrange("p g d -> p (g d)")

        with nc.Block() as block:
            xt = work[0:D, 0:2 * GROUP]
            tab = work[:, 512:512 + 2 * 2 * ROW0]
            erb = work[:, 1536:1536 + 8]

            @block.sync
            def _(sp):
                with sp.Fori(0, NG // 2) as j:
                    for b in range(2):
                        sp.wait_ge(S["xt_ready"], 2 * j + b + 1)
                        sp.dma_start(xt[:, b * GROUP:(b + 1) * GROUP],
                                     a["x_cols"][:, bass.ds((2 * j + b) * GROUP, GROUP)]).then_inc(S["loaded"], 16)
                        sp.wait_ge(S["loaded"], (2 * j + b) * 16 + 16)
                        sp.sem_inc(S["chunk_in"], 1)

            @block.tensor
            def _(pe):
                from_one(pe, "xt_ready")
                pe.sem_inc(S["xt_ready"], 1)
                with pe.Fori(0, NG // 2) as j:
                    for b in range(2):
                        pe.wait_ge(S["chunk_in"], 2 * j + b + 1)
                        pe.wait_ge(S["out_free"], 2 * j + b + 1)
                        for h in range(2):
                            mm = nc.tensor.matmul(psum[b][:, h * ROW0:(h + 1) * ROW0],
                                                  xt[:, b * GROUP + h:(b + 1) * GROUP:2], w("fcx", D),
                                                  start=True, stop=True)
                        mm.then_inc(S["hid_ready"], 1)
                        pe.wait_ge(S["hid_ready"], 2 * j + b + 1)
                        pe.sem_inc(S["xt_ready"], 1)

            @block.vector
            def _(dve):
                from_one(dve, "out_free")
                dve.sem_inc(S["out_free"], 1)
                with dve.Fori(0, NG // 2) as j:
                    for b in range(2):
                        t = tab[:, b * 2 * ROW0:(b + 1) * 2 * ROW0]
                        dve.wait_ge(S["hid_ready"], 2 * j + b + 1)
                        dve.wait_ge(S["stored"], 32 * (2 * j + b) + 1)
                        nc.vector.tensor_copy(t, psum[b][:, 0:2 * ROW0]).then_inc(S["tab_copied"], 1)
                        nc.vector.tensor_copy(
                            erb[:, 4 * b:4 * b + 4].rearrange("p (a s) -> p a s", a=2),
                            psum[b][:, 0:2 * ROW0].rearrange("p (a d) -> p a d", a=2)[:, :, HD + 2:ROW0],
                        ).then_inc(S["out_free"], 1)

            @block.scalar
            def _(act):
                from_one(act, "stored")
                act.sem_inc(S["stored"], 32)
                with act.Fori(0, NG // 2) as j:
                    for b in range(2):
                        act.wait_ge(S["tab_copied"], 2 * j + b + 1)
                        act.dma_start(group_rows(table0, 2 * j + b, ROW0),
                                      tab[:, b * 2 * ROW0:(b + 1) * 2 * ROW0]).then_inc(S["tab_stored"], 16)
                        act.wait_ge(S["out_free"], 2 * j + b + 3)
                        act.dma_start(group_rows(er_table, 2 * j + b, 2),
                                      erb[:, 4 * b:4 * b + 4]).then_inc(S["tab_stored"], 16)
                        act.wait_ge(S["tab_stored"], 32 * (2 * j + b) + 32)
                        act.sem_inc(S["stored"], 32)
        new_phase()

        def gathers(table, width, idx, er=False):
            pool = nc.gpsimd
            per = CHUNK * SLOTS
            with pool.Fori(0, LOOPS // 2) as jj:
                for half in range(2):
                    j = 2 * jj + half
                    if er:
                        pool.tensor_copy(dst_now[:, half, :], dst_u[:, bass.ds(j * per, per)])
                    pool.tensor_copy(idx_now[:, half, :], idx[:, bass.ds(j * per, per)]).then_inc(S["idx_ready"], 1)
                    pool.wait_ge(S["idx_ready"], j + 1)
                    for q in range(SLOTS):
                        hold(pool, S["slot_free"], SLOTS * j + q + 1)
                        for k in range(CHUNK):
                            c = q * CHUNK + k
                            pool.indirect_dma_start(
                                out=ring[:, c * width:(c + 1) * width], out_offset=None, in_=table,
                                in_offset=bass.IndirectOffsetOnAxis(ap=idx_now[:, half, c:c + 1], axis=0),
                            ).then_inc(S[f"gathered_s{q}"], 16)
                            if er:
                                pool.indirect_dma_start(
                                    out=er_ring[:, 2 * c:2 * c + 2], out_offset=None, in_=er_table[:, :],
                                    in_offset=bass.IndirectOffsetOnAxis(ap=dst_now[:, half, c:c + 1], axis=0),
                                ).then_inc(S[f"gathered_s{q}"], 16)

        with nc.Block() as block:
            gs = work[0:D, 0:512]
            soft_u = work[:, 512:1024]
            soft_r = work[:, 1024:1536]
            m4 = work[:, 1536:2048]
            m4v = m4.rearrange("p (k d) -> p k d", k=CHUNK)
            er4 = small[:, 0:8].rearrange("p (k s) -> p k s", s=2)
            msg_v = msg[:, :].rearrange("p (t d) -> p t d", d=MW)
            spill_v = spill.rearrange("p (t d) -> p t d", d=D)

            @block.gpsimd
            def _(pool):
                gathers(table0[:, :], ROW0, src_u, er=True)

            @block.sync
            def _(sp):
                sp.sem_inc(S["slot_free"], SLOTS)
                with sp.Fori(0, NCH) as c:
                    sp.wait_ge(S["hid_free"], c + 1)
                    sp.dma_start(gs, a["gs_cols"][:, bass.ds(c * 512, 512)]).then_inc(S["chunk_in"], 16)

            @block.tensor
            def _(pe):
                from_one(pe, "hid_free", "filt_ready")
                with pe.Fori(0, NCH) as c:
                    pe.wait_ge(S["chunk_in"], 16 * c + 16)
                    pe.wait_ge(S["evac"], c + 1)
                    nc.tensor.matmul(psum[0][:, :], w("filt_w1", D), gs, start=True, stop=True).then_inc(S["hid_free"], 1)
                    pe.wait_ge(S["soft_done"], c + 2)
                    pe.wait_ge(S["filt_free"], c + 1)
                    for k in range(CHUNK):
                        nc.tensor.matmul(psum[1][:, k * P:(k + 1) * P], orow[:, :], row("filt_b2"), start=True, stop=False)
                        mm = nc.tensor.matmul(psum[1][:, k * P:(k + 1) * P], soft_r[:, k * P:(k + 1) * P],
                                              w("filt_w2", P), start=False, stop=True)
                    mm.then_inc(S["filt_ready"], 1)

            @block.scalar
            def _(act):
                from_one(act, "slot_used", "head_copied")
                with act.Fori(0, NCH) as c:
                    act.wait_ge(S["evac"], c + 2)
                    act.wait_ge(S["soft_done"], c + 1)
                    nc.scalar.activation(soft_u, soft_r, ACT.Abs).then_inc(S["soft_abs"], 1)
                    act.wait_ge(S["soft_abs"], c + 1)
                    nc.scalar.activation(soft_u, soft_u, ACT.Exp, scale=-1.0).then_inc(S["soft_exp"], 1)
                    act.wait_ge(S["soft_exp"], c + 1)
                    nc.scalar.activation(soft_u, soft_u, ACT.Ln, bias=bias[:, ONE:ONE + 1]).then_inc(S["soft_ln"], 1)
                    act.wait_ge(S["filt_free"], c + 2)
                    nc.scalar.copy(msg_v[:, bass.ds(c * CHUNK, CHUNK), 0:D], m4v[:, :, 0:D]).then_inc(S["head_copied"], 1)
                    act.dma_start(spill_v[:, bass.ds(c * CHUNK, CHUNK), :], m4v[:, :, D:HD]).then_inc(S["placed"], 16)
                    act.wait_ge(S["placed"], 16 * c + 16)
                    act.wait_ge(S["head_copied"], c + 2)
                    act.sem_inc(S["slot_used"], 1)

            @block.vector
            def _(dve):
                from_one(dve, "soft_done", "filt_free", "evac")
                v = nc.vector
                v.memset(msg_v[:, 0:T, D:MW], 1.0)
                with dve.Fori(0, LOOPS) as j:
                    for q in range(SLOTS):
                        c = SLOTS * j + q
                        slot = ring[:, q * CHUNK * ROW0:(q + 1) * CHUNK * ROW0].rearrange("p (k d) -> p k d", d=ROW0)
                        ers = er_ring[:, q * CHUNK * 2:(q + 1) * CHUNK * 2].rearrange("p (k s) -> p k s", s=2)
                        dve.wait_ge(S["hid_free"], c + 2)
                        dve.wait_ge(S["filt_ready"], c + 1)
                        v.tensor_scalar(soft_r, psum[0][:, :], bias[:, B1:B1 + 1], None, ALU.add).then_inc(S["evac"], 1)
                        dve.wait_ge(S["soft_ln"], c + 1)
                        v.scalar_tensor_tensor(soft_r, soft_r, 0.0, soft_u, ALU.max, ALU.add).then_inc(S["soft_done"], 1)
                        dve.wait_ge(S[f"gathered_s{q}"], (j + 1) * (32 * CHUNK) + gathered_before[0])
                        v.tensor_tensor(er4, slot[:, :, HD:HD + 2], ers, ALU.add).then_inc(S["step"], 1)
                        dve.wait_ge(S["step"], 2 * c + 1)
                        v.scalar_tensor_tensor(exw[:, bass.ds(c * CHUNK, CHUNK), :], er4, 0.2, er4, ALU.mult,
                                               ALU.max).then_inc(S["step"], 1)
                        dve.wait_ge(S["step"], 2 * c + 2)
                        dve.wait_ge(S["filt_ready"], c + 2)
                        dve.wait_ge(S["slot_used"], c + 1)
                        for k in range(CHUNK):
                            ins = v.scalar_tensor_tensor(
                                m4v[:, k, :], psum[1][:, k * P:(k + 1) * P], cut[:, bass.ds(c * CHUNK + k, 1)],
                                slot[:, k, 0:HD], ALU.mult, ALU.mult)
                        ins.then_inc(S["filt_free"], 1)
                        dve.wait_ge(S["filt_free"], c + 2)
                        dve.sem_inc(S["slot_free"], 1)
        new_phase()
        gathered_before[0] += LOOPS * 32 * CHUNK

        def turn_scores(to_flat, flat):
            with nc.Block() as block:
                tiles_at = lambda i: work[0:Q, 128 * i:128 * i + P]

                @block.tensor
                def _(pe):
                    for i in range(8):
                        h, b = divmod(i, 4)
                        if to_flat:
                            mm = nc.tensor.transpose(psum[i][0:Q, 0:P], exw[:, b * Q:(b + 1) * Q, h], ident[:, :])
                        else:
                            pe.wait_ge(S["loaded"], 16 * 8)
                            mm = nc.tensor.transpose(psum[i][:, 0:Q], tiles_at(i), ident[0:Q, 0:Q])
                        mm.then_inc(S["turned"], 1)

                @block.vector
                def _(dve):
                    for i in range(8):
                        h, b = divmod(i, 4)
                        dve.wait_ge(S["turned"], i + 1)
                        if to_flat:
                            nc.vector.tensor_copy(tiles_at(i), psum[i][0:Q, 0:P]).then_inc(S["made"], 1)
                        else:
                            nc.vector.tensor_tensor(exw[:, b * Q:(b + 1) * Q, h], exw[:, b * Q:(b + 1) * Q, h],
                                                    psum[i][:, 0:Q], ALU.subtract).then_inc(S["made"], 1)

                @block.scalar
                def _(act):
                    if not to_flat:
                        act.wait_ge(S["made"], 8)
                        nc.scalar.activation(exw[:, 0:T, :], exw[:, 0:T, :], ACT.Exp)

                @block.sync
                def _(sp):
                    for i in range(8):
                        h, b = divmod(i, 4)
                        view = flat[h, b * Q * P:(b + 1) * Q * P].rearrange("(q p) -> q p", p=P)
                        if to_flat:
                            sp.wait_ge(S["made"], i + 1)
                            sp.dma_start(view, tiles_at(i)).then_inc(S["written"], 16)
                        else:
                            sp.dma_start(tiles_at(i), view).then_inc(S["loaded"], 16)
                    if to_flat:
                        sp.wait_ge(S["written"], 16 * 8)
            new_phase()

        def flat_scan(source, mask, target, backward):
            with nc.Block() as block:
                vals = work[0:2, 0:SC]
                mbuf = ring[0:2, 0:SC]
                carry = sloop[0:2, 0:1]
                steps = EP // SC
                NEG = -1.0 if not backward else 1.0

                def at_(c):
                    return (steps - 1 - c) * SC if backward else c * SC

                @block.sync
                def _(sp):
                    with sp.Fori(0, steps) as c:
                        hold(sp, S["scan_done"], 2 * c + 1)
                        sp.dma_start(vals, source[:, bass.ds(at_(c), SC)]).then_inc(S["loaded"], 16)
                        sp.dma_start(mbuf, mask[0:1, bass.ds(at_(c), SC)].broadcast_to([2, SC])).then_inc(S["loaded"], 16)
                        sp.wait_ge(S["scan_done"], 2 * c + 3)
                        sp.dma_start(target[:, bass.ds(at_(c), SC)], vals).then_inc(S["written"], 16)
                        hold(sp, S["written"], 16 * c + 16)

                @block.vector
                def _(dve):
                    from_one(dve, "scan_done")
                    v = nc.vector
                    v.memset(carry, 0.0).then_inc(S["step"], 1)
                    dve.wait_ge(S["step"], 1)
                    with dve.Fori(0, steps) as c:
                        dve.wait_ge(S["loaded"], 32 * c + 32)
                        if not backward:
                            v.tensor_scalar(mbuf, mbuf, -1.0, None, ALU.mult).then_inc(S["made"], 1)
                            dve.wait_ge(S["made"], c + 1)
                        d0, d1 = (mbuf[:, SC - 1::-1], vals[:, SC - 1::-1]) if backward else (mbuf, vals)
                        v.tensor_tensor_scan(d1, d0, d1, carry, ALU.add, ALU.max).then_inc(S["scan_done"], 1)
                        dve.wait_ge(S["scan_done"], 2 * c + 2)
                        end = vals[:, 0:1] if backward else vals[:, SC - 1:SC]
                        v.tensor_copy(carry, end).then_inc(S["scan_done"], 1)
                        dve.wait_ge(S["scan_done"], 2 * c + 3)
            new_phase()

        turn_scores(True, flat_e)
        flat_scan(flat_e, same_prev, flat_f, False)
        flat_scan(flat_f, same_next, flat_m, True)
        turn_scores(False, flat_m)

        AGG = psum[0]

        def load_run(eng, g):
            start = eng.value_load(runs[0:1, bass.ds(g * 4, 1)], min_val=0, max_val=T - 1)
            end = eng.value_load(runs[0:1, bass.ds(g * 4 + 1, 1)], min_val=2, max_val=T + 1)
            offset = eng.value_load(runs[0:1, bass.ds(g * 4 + 2, 1)], min_val=0, max_val=T + 2 * NG)
            return start, end, offset

        def reduce_pe(pe, g, width, stride, live):
            start, end, offset = load_run(pe, g)
            if live:
                pe.wait_ge(S["msgs_ready"], (end + (CHUNK - 1)) >> 2)
            pe.wait_ge(S["agg_taken"], g + 1)
            nc.tensor.matmul(AGG[:, 0:2 * width], zrow[:, 0:P], zrow[:, 0:2 * width], start=True, stop=False,
                             skip_group_check=True)
            with pe.Fori(start, end, 2) as e:
                for k in range(2):
                    pe.wait_ge(S["sel_ready"], e + offset + (k + 1))
                    for h in range(2):
                        mm = nc.tensor.matmul(AGG[:, h * width:(h + 1) * width], sel[:, k, h * P:(h + 1) * P],
                                              msg[:, bass.ds((e + k) * stride, width)],
                                              start=False, stop=False, skip_group_check=True)
                    mm.then_inc(S["sel_free"], 1)
            nc.tensor.matmul(AGG[:, 0:2 * width], zrow[:, 0:P], zrow[:, 0:2 * width], start=False, stop=True,
                             skip_group_check=True).then_inc(S["agg_ready"], 1)

        def select_dve(dve, g, weight):
            start, end, offset = load_run(dve, g)
            nc.vector.tensor_scalar(node_ids[:, :], lane[:, :], gbase[:, bass.ds(g, 1)], None,
                                    ALU.add).then_inc(S["rows_ready"], 1)
            hold(dve, S["rows_ready"], g + 1)
            with dve.Fori(start, end, 2) as first:
                for k in range(2):
                    e = first + k
                    dve.wait_ge(S["sel_free"], e + offset + 1)
                    if weight is None:
                        ins = nc.vector.tensor_scalar(sel[:, k, :], node_ids[:, :], dst_f[:, bass.ds(e, 1)], None,
                                                      ALU.is_equal)
                    else:
                        ins = nc.vector.tensor_scalar(sel[:, k, :], node_ids[:, :], dst_f[:, bass.ds(e, 1)], weight(e),
                                                      ALU.is_equal, ALU.mult)
                    ins.then_inc(S["sel_ready"], 1)

        def place_messages(sp):
            sp.sem_inc(S["slot_free"], SLOTS)
            with sp.Fori(0, LOOPS) as j:
                for q in range(SLOTS):
                    c = SLOTS * j + q
                    sp.wait_ge(S[f"gathered_s{q}"], (j + 1) * (16 * CHUNK) + gathered_before[0])
                    sp.dma_start(msg[:, bass.ds(c * (CHUNK * D), CHUNK * D)],
                                 ring[:, q * CHUNK * D:(q + 1) * CHUNK * D]).then_inc(S["placed"], 16)
                    sp.wait_ge(S["placed"], c * 16 + 16)
                    sp.sem_inc(S["slot_free"], 1)
                    sp.sem_inc(S["msgs_ready"], 1)
            sp.sem_inc(S["msgs_ready"], 1)

        def nothing(g):
            pass

        def groups(eng, reduce, take, node):
            reduce(0)
            with eng.Fori(0, NG - 1) as g:
                take(g)
                reduce(g + 1)
                node(g)
            take(NG - 1)
            node(NG - 1)

        nin = work[:, 0:2 * HD]
        agg = work[:, 256:256 + 2 * MW]
        vs = work[:, 512:512 + HD]
        xn = work[:, 640:640 + HD]
        vt = work[:, 768:768 + GROUP]
        ht = work[:, 1024:1024 + GROUP]
        ot = work[:, 1280:1280 + HD]
        soft_a = work[:, 1536:1536 + GROUP]
        soft_b = work[:, 1792:1792 + GROUP]
        hb = work[:, 2048:2048 + 2 * HD]
        sb_ = work[:, 2304:2304 + HD]
        cat = work[:, 2560:2560 + GROUP]
        st = small[:, 0:12]
        mv = small[:, 16:20]
        rstd = small[:, 20:22]
        lnv = small[:, 22:24]

        def halves(t):
            return t.rearrange("p (a d) -> p a d", a=2)

        def norm_dve(dve, g, src, dst):
            v = nc.vector
            for h in range(2):
                ins = v.bn_stats(st[:, 6 * h:6 * h + 6], halves(src)[:, h, :])
            ins.then_inc(S["ln_step"], 1)
            hold(dve, S["ln_step"], 2 * g + 1)
            for h in range(2):
                ins = v.bn_aggr(mv[:, 2 * h:2 * h + 2], st[:, 6 * h:6 * h + 6])
            ins.then_inc(S["stat_ready"], 1)
            dve.wait_ge(S["rstd_ready"], g + 1)
            for h in range(2):
                ins = v.tensor_scalar(halves(dst)[:, h, :], halves(src)[:, h, :], mv[:, 2 * h:2 * h + 1],
                                      rstd[:, h:h + 1], ALU.subtract, ALU.mult)
            ins.then_inc(S["ln_step"], 1)
            dve.wait_ge(S["ln_step"], 2 * g + 2)

        def norm_act(act, g):
            act.wait_ge(S["stat_ready"], g + 1)
            nc.scalar.activation(lnv, mv.rearrange("p (a s) -> p a s", s=2)[:, :, 1], ACT.Ln,
                                 bias=bias[:, EPSC:EPSC + 1]).then_inc(S["soft2_ln"], 1)
            act.wait_ge(S["soft2_ln"], g + 1)
            nc.scalar.activation(rstd, lnv, ACT.Exp, scale=-0.5).then_inc(S["rstd_ready"], 1)

        def take_head(dve, g, dst):
            v = nc.vector
            dve.wait_ge(S["agg_ready"], g + 1)
            v.tensor_copy(agg, AGG[:, 0:2 * MW]).then_inc(S["agg_taken"], 1)
            dve.wait_ge(S["agg_taken"], g + 2)
            av = halves(agg)
            v.tensor_scalar(small[:, 24:26], av[:, :, D], 1e-16, None, ALU.max).then_inc(S["evac"], 1)
            dve.wait_ge(S["evac"], 2 * g + 1)
            v.reciprocal(small[:, 26:28], small[:, 24:26]).then_inc(S["evac"], 1)
            dve.wait_ge(S["evac"], 2 * g + 2)
            for h in range(2):
                ins = v.tensor_scalar(dst[h], av[:, h, 0:D], small[:, 26 + h:27 + h], None, ALU.mult)
            return ins

        def store_rows(act, g, table, tile, width):
            act.dma_start(group_rows(table, g, width), tile).then_inc(S["out_ready"], 16)

        with nc.Block() as block:
            @block.tensor
            def _(pe):
                pe.sem_inc(S["sel_free"], 2)
                groups(pe, lambda g: reduce_pe(pe, g, MW, MW, False), nothing, nothing)

            @block.vector
            def _(dve):
                from_one(dve, "agg_taken")
                def take(g):
                    dve.wait_ge(S["stored"], g + 1)
                    take_head(dve, g, [halves(vs)[:, h, :] for h in range(2)]).then_inc(S["vsum"], 1)
                groups(dve, lambda g: select_dve(dve, g, lambda e: exw[:, bass.ds(e, 1), 0]), take, nothing)

            @block.scalar
            def _(act):
                from_one(act, "stored")
                with act.Fori(0, NG) as g:
                    act.wait_ge(S["vsum"], g + 1)
                    store_rows(act, g, head0, vs, D)
                    act.wait_ge(S["out_ready"], 16 * g + 16)
                    act.sem_inc(S["stored"], 1)
        new_phase()

        with nc.Block() as block:
            x1t = work[0:D, 2816:2816 + GROUP]
            msg_v = msg[:, :].rearrange("p (t d) -> p t d", d=MW)

            @block.sync
            def _(sp):
                from_one(sp, "stored")
                sp.dma_start(msg_v[:, 0:T, 0:D], spill.rearrange("p (t d) -> p t d", d=D)).then_inc(S["placed"], 16)
                sp.wait_ge(S["placed"], 16)
                sp.sem_inc(S["msgs_ready"], T // CHUNK + 1)
                with sp.Fori(0, NG) as g:
                    sp.wait_ge(S["xn_ready"], g + 1)
                    sp.dma_start(nin[:, 0:HD], group_rows(head0, g, D)).then_inc(S["node_in"], 16)
                    sp.dma_start(nin[:, HD:2 * HD], group_rows(a["x_rows"], g, D)).then_inc(S["node_in"], 16)
                    sp.wait_ge(S["xn_ready"], g + 2)
                    sp.dma_start(group_rows(x1, g, D), xn).then_inc(S["out_ready"], 16)
                    sp.wait_ge(S["tab_copied"], 2 * g + 2)
                    sp.dma_start(group_rows(y_table, g, D), hb[:, 0:HD]).then_inc(S["out_ready"], 16)
                    sp.dma_start(group_rows(yb_rows, g, D), hb[:, HD:2 * HD]).then_inc(S["out_ready"], 16)
                    sp.wait_ge(S["out_ready"], 48 * g + 48)
                    sp.sem_inc(S["stored"], 1)

            @block.tensor
            def _(pe):
                from_one(pe, "turned_v")
                pe.sem_inc(S["sel_free"], 2)

                def node(g):
                    hold(pe, S["soft_done"], g + 2)
                    for h in range(2):
                        mm = nc.tensor.transpose(psum[1][:, h * P:(h + 1) * P], cat[:, h * P:(h + 1) * P], ident[:, :])
                    mm.then_inc(S["turned_v"], 1)
                    hold(pe, S["vt_ready"], g + 1)
                    nc.tensor.matmul(psum[2][0:D, 0:GROUP], w("mlp_w1", P), vt, start=True, stop=True).then_inc(S["hid_ready"], 1)
                    pe.wait_ge(S["soft2_done"], g + 1)
                    for h in range(2):
                        nc.tensor.matmul(psum[3][:, h * D:(h + 1) * D], orow[:, :], row("mlp_b2"), start=True, stop=False)
                        mm = nc.tensor.matmul(psum[3][:, h * D:(h + 1) * D], ht[0:D, h * P:(h + 1) * P],
                                              w("mlp_w2", D), start=False, stop=True)
                    mm.then_inc(S["act_ready"], 1)
                    hold(pe, S["xn_ready"], g + 2)
                    for h in range(2):
                        mm = nc.tensor.transpose(psum[4][0:D, h * P:(h + 1) * P], halves(xn)[:, h, :], ident[:, :])
                    mm.then_inc(S["turned"], 1)
                    pe.wait_ge(S["xt_ready"], g + 2)
                    for h in range(2):
                        nc.tensor.matmul(psum[5][:, h * HD:(h + 1) * HD], orow[:, :], row("yb"), start=True, stop=False)
                        mm = nc.tensor.matmul(psum[5][:, h * HD:(h + 1) * HD], x1t[:, h * P:(h + 1) * P],
                                              w("W1W1", D), start=False, stop=True)
                    mm.then_inc(S["tab_ready"], 1)
                groups(pe, lambda g: reduce_pe(pe, g, MW, MW, True), nothing, node)

            @block.vector
            def _(dve):
                from_one(dve, "agg_taken", "xn_ready", "soft_done")
                v = nc.vector

                def take(g):
                    cv = cat.rearrange("p (a s d) -> p a s d", a=2, s=2)
                    dve.wait_ge(S["turned_v"], g + 1)
                    take_head(dve, g, [cv[:, h, 1, :] for h in range(2)]).then_inc(S["res_ready"], 1)
                    dve.wait_ge(S["node_in"], 32 * g + 32)
                    v.tensor_copy(cv[:, :, 0, :], halves(nin[:, 0:HD])).then_inc(S["vsum"], 1)

                def node(g):
                    dve.wait_ge(S["res_ready"], g + 1)
                    dve.wait_ge(S["soft_ln"], g + 1)
                    v.scalar_tensor_tensor(cat, cat, 0.0, soft_a, ALU.max, ALU.add).then_inc(S["soft_done"], 1)
                    dve.wait_ge(S["hid_ready"], g + 1)
                    v.tensor_scalar(ht[0:D, :], psum[2][0:D, 0:GROUP], bias[0:D, MB1:MB1 + 1], None,
                                    ALU.add).then_inc(S["step"], 1)
                    dve.wait_ge(S["soft_exp"], 3 * g + 3)
                    v.scalar_tensor_tensor(ht[0:D, :], ht[0:D, :], 0.0, soft_b[0:D, :], ALU.max, ALU.add).then_inc(S["soft2_done"], 1)
                    dve.wait_ge(S["act_ready"], g + 1)
                    v.tensor_tensor(vs, psum[3][:, 0:HD], nin[:, HD:2 * HD], ALU.add).then_inc(S["chunk_in"], 1)
                    dve.wait_ge(S["chunk_in"], g + 1)
                    dve.wait_ge(S["stored"], g + 1)
                    norm_dve(dve, g, vs, xn)
                    dve.sem_inc(S["xn_ready"], 1)
                groups(dve, lambda g: select_dve(dve, g, lambda e: exw[:, bass.ds(e, 1), 1]), take, node)

            @block.scalar
            def _(act):
                from_one(act, "xt_ready")
                with act.Fori(0, NG) as g:
                    act.wait_ge(S["vsum"], g + 1)
                    act.wait_ge(S["res_ready"], g + 1)
                    act.wait_ge(S["soft_done"], g + 1)
                    nc.scalar.activation(soft_a, cat, ACT.Abs).then_inc(S["soft_abs"], 1)
                    act.wait_ge(S["soft_abs"], g + 1)
                    nc.scalar.activation(soft_a, soft_a, ACT.Exp, scale=-1.0).then_inc(S["soft2_exp"], 1)
                    act.wait_ge(S["soft2_exp"], g + 1)
                    nc.scalar.activation(soft_a, soft_a, ACT.Ln, bias=bias[:, ONE:ONE + 1]).then_inc(S["soft_ln"], 1)
                    act.wait_ge(S["turned_v"], g + 2)
                    nc.scalar.copy(vt, psum[1][:, 0:GROUP]).then_inc(S["vt_ready"], 1)
                    act.wait_ge(S["step"], g + 1)
                    u = soft_b[0:D, :]
                    nc.scalar.activation(u, ht[0:D, :], ACT.Abs).then_inc(S["soft_exp"], 1)
                    act.wait_ge(S["soft_exp"], 3 * g + 1)
                    nc.scalar.activation(u, u, ACT.Exp, scale=-1.0).then_inc(S["soft_exp"], 1)
                    act.wait_ge(S["soft_exp"], 3 * g + 2)
                    nc.scalar.activation(u, u, ACT.Ln, bias=bias[0:D, ONE:ONE + 1]).then_inc(S["soft_exp"], 1)
                    norm_act(act, g)
                    act.wait_ge(S["turned"], g + 1)
                    nc.scalar.copy(x1t, psum[4][0:D, 0:GROUP]).then_inc(S["xt_ready"], 1)
                    act.wait_ge(S["tab_ready"], g + 1)
                    nc.scalar.copy(halves(hb[:, 0:HD]), halves(psum[5][:, 0:2 * HD])[:, :, 0:D]).then_inc(S["tab_copied"], 1)
                    nc.scalar.copy(halves(hb[:, HD:2 * HD]), halves(psum[5][:, 0:2 * HD])[:, :, D:HD]).then_inc(S["tab_copied"], 1)
        new_phase()

        with nc.Block() as block:
            mask = work[0:D, 0:512]
            scn = work[0:D, 512:1024]
            carry = sloop[0:D, 1:2]
            msg_v = msg[:, :].rearrange("p (t d) -> p t d", d=MW)

            @block.gpsimd
            def _(pool):
                gathers(y_table[:, :], D, src_u)

            @block.sync
            def _(sp):
                with sp.Fori(0, NCH) as c:
                    sp.wait_ge(S["scan_done"], 2 * c + 1)
                    sp.dma_start(mask, same_prev[0:1, bass.ds(c * 512, 512)].broadcast_to([D, 512])).then_inc(S["loaded"], 16)

            @block.tensor
            def _(pe):
                from_one(pe, "back_ready")
                pe.sem_inc(S["slot_free"], SLOTS)
                with pe.Fori(0, LOOPS) as j:
                    for q in range(SLOTS):
                        c = SLOTS * j + q
                        pe.wait_ge(S[f"gathered_s{q}"], (j + 1) * (16 * CHUNK) + gathered_before[0])
                        hold(pe, S["scan_done"], 2 * c + 1)
                        for k in range(CHUNK):
                            mm = nc.tensor.transpose(psum[1][0:D, k * P:(k + 1) * P],
                                                     ring[:, (q * CHUNK + k) * D:(q * CHUNK + k + 1) * D], ident[:, :])
                        mm.then_inc(S["turned"], 1)
                        pe.wait_ge(S["turned"], c + 1)
                        pe.sem_inc(S["slot_free"], 1)
                        pe.wait_ge(S["scan_done"], 2 * c + 2)
                        hold(pe, S["head_copied"], c + 1)
                        for k in range(CHUNK):
                            mm = nc.tensor.transpose(psum[2][:, k * D:(k + 1) * D], scn[:, k * P:(k + 1) * P],
                                                     ident[0:D, 0:D])
                        mm.then_inc(S["back_ready"], 1)

            @block.vector
            def _(dve):
                from_one(dve, "scan_done")
                v = nc.vector
                v.memset(carry, 0.0).then_inc(S["step"], 1)
                dve.wait_ge(S["step"], 1)
                with dve.Fori(0, NCH) as c:
                    dve.wait_ge(S["loaded"], 16 * c + 16)
                    dve.wait_ge(S["turned"], c + 1)
                    dve.wait_ge(S["back_ready"], c + 1)
                    v.tensor_tensor_scan(scn, mask, psum[1][0:D, :], carry, ALU.add, ALU.min).then_inc(S["scan_done"], 1)
                    dve.wait_ge(S["scan_done"], 2 * c + 2)
                    v.tensor_copy(carry, scn[:, 511:512]).then_inc(S["scan_done"], 1)
                    dve.wait_ge(S["scan_done"], 2 * c + 3)

            @block.scalar
            def _(act):
                from_one(act, "head_copied")
                with act.Fori(0, NCH) as c:
                    act.wait_ge(S["back_ready"], c + 2)
                    nc.scalar.copy(msg_v[:, bass.ds(c * CHUNK, CHUNK), 0:D],
                                   psum[2][:, 0:CHUNK * D].rearrange("p (k d) -> p k d", d=D)).then_inc(S["head_copied"], 1)
        new_phase()
        gathered_before[0] += LOOPS * 16 * CHUNK

        with nc.Block() as block:
            @block.sync
            def _(sp):
                from_one(sp, "stored")
                with sp.Fori(0, NG) as g:
                    sp.wait_ge(S["xn_ready"], g + 1)
                    sp.dma_start(nin[:, 0:HD], group_rows(yb_rows, g, D)).then_inc(S["node_in"], 16)
                    sp.dma_start(nin[:, HD:2 * HD], group_rows(x1, g, D)).then_inc(S["node_in"], 16)
                    sp.wait_ge(S["xn_ready"], g + 2)
                    sp.dma_start(group_rows(x2, g, D), xn).then_inc(S["out_ready"], 16)
                    sp.wait_ge(S["out_ready"], 16 * g + 16)
                    sp.sem_inc(S["stored"], 1)

            @block.tensor
            def _(pe):
                pe.sem_inc(S["sel_free"], 2)
                groups(pe, lambda g: reduce_pe(pe, g, MW, MW, False), nothing, nothing)

            @block.vector
            def _(dve):
                from_one(dve, "agg_taken", "xn_ready")
                v = nc.vector

                def take(g):
                    dve.wait_ge(S["agg_ready"], g + 1)
                    v.tensor_copy(agg, AGG[:, 0:2 * MW]).then_inc(S["agg_taken"], 1)
                    dve.wait_ge(S["agg_taken"], g + 2)

                def node(g):
                    av = halves(agg)
                    dve.wait_ge(S["node_in"], 32 * g + 32)
                    v.tensor_tensor(halves(vs), halves(nin[:, 0:HD]), av[:, :, 0:D], ALU.subtract).then_inc(S["evac"], 1)
                    dve.wait_ge(S["evac"], 3 * g + 1)
                    v.scalar_tensor_tensor(ot, vs, 0.01, vs, ALU.mult, ALU.max).then_inc(S["evac"], 1)
                    dve.wait_ge(S["evac"], 3 * g + 2)
                    for h in range(2):
                        ins = v.scalar_tensor_tensor(halves(vs)[:, h, :], halves(ot)[:, h, :], av[:, h, D:MW],
                                                     halves(nin[:, HD:2 * HD])[:, h, :], ALU.mult, ALU.add)
                    ins.then_inc(S["evac"], 1)
                    dve.wait_ge(S["evac"], 3 * g + 3)
                    dve.wait_ge(S["stored"], g + 1)
                    norm_dve(dve, g, vs, xn)
                    dve.sem_inc(S["xn_ready"], 1)
                groups(dve, lambda g: select_dve(dve, g, lambda e: last_w[:, bass.ds(e, 1)]), take, node)

            @block.scalar
            def _(act):
                with act.Fori(0, NG) as g:
                    norm_act(act, g)
        new_phase()

        def clear_tail():
            with nc.Block() as block:
                @block.vector
                def _(dve):
                    nc.vector.memset(msg[:, T * D:(T + 2) * D], 0.0)
            new_phase()

        clear_tail()

        def gin(table, target, wa, wb, hidden, ba, bb, last):
            with nc.Block() as block:
                r2t = work[:, 2816:2816 + GROUP]

                @block.gpsimd
                def _(pool):
                    gathers(table[:, :], D, src_u)

                @block.sync
                def _(sp):
                    place_messages(sp)

                @block.tensor
                def _(pe):
                    from_one(pe, "turned_v")
                    pe.sem_inc(S["sel_free"], 2)

                    def node(g):
                        hold(pe, S["vsum"], g + 1)
                        for h in range(2):
                            mm = nc.tensor.transpose(psum[1][0:D, h * P:(h + 1) * P], halves(vs)[:, h, :], ident[:, :])
                        mm.then_inc(S["turned_v"], 1)
                        hold(pe, S["vt_ready"], g + 1)
                        nc.tensor.matmul(psum[2][0:hidden, 0:GROUP], w(wa, D), vt[0:D, :], start=True,
                                         stop=True).then_inc(S["hid_ready"], 1)
                        pe.wait_ge(S["act_ready"], g + 1)
                        for h in range(2):
                            nc.tensor.matmul(psum[3][:, h * D:(h + 1) * D], orow[:, :], row(bb), start=True, stop=False)
                            mm = nc.tensor.matmul(psum[3][:, h * D:(h + 1) * D], ht[0:hidden, h * P:(h + 1) * P],
                                                  w(wb, hidden), start=False, stop=True)
                        mm.then_inc(S["res_ready"], 1)
                        if last:
                            relation_tables_pe(pe, g, w("R0", D), row("rb0"))
                    groups(pe, lambda g: reduce_pe(pe, g, D, D, True), nothing, node)

                @block.vector
                def _(dve):
                    from_one(dve, "agg_taken", "xn_ready")
                    v = nc.vector

                    def take(g):
                        dve.wait_ge(S["node_in"], (32 if last else 16) * (g + 1))
                        dve.wait_ge(S["agg_ready"], g + 1)
                        dve.wait_ge(S["turned_v"], g + 1)
                        v.tensor_tensor(vs, AGG[:, 0:HD], nin[:, 0:HD], ALU.add).then_inc(S["vsum"], 1)
                        dve.wait_ge(S["vsum"], g + 1)
                        dve.sem_inc(S["agg_taken"], 1)

                    def node(g):
                        if last:
                            dve.wait_ge(S["res_ready"], g + 1)
                            v.tensor_tensor(ot, psum[3][:, 0:HD], nin[:, HD:2 * HD], ALU.add).then_inc(S["evac"], 1)
                            dve.wait_ge(S["evac"], g + 1)
                            dve.wait_ge(S["stored"], g + 1)
                            norm_dve(dve, g, ot, xn)
                            dve.sem_inc(S["xn_ready"], 1)
                    groups(dve, lambda g: select_dve(dve, g, lambda e: ew[:, bass.ds(e, 1)]), take, node)

                @block.scalar
                def _(act):
                    from_one(act, "stored", "xt_ready")
                    with act.Fori(0, NG) as g:
                        act.dma_start(nin[:, 0:HD], group_rows(table, g, D)).then_inc(S["node_in"], 16)
                        if last:
                            act.dma_start(nin[:, HD:2 * HD], group_rows(x2, g, D)).then_inc(S["node_in"], 16)
                        act.wait_ge(S["turned_v"], g + 2)
                        nc.scalar.copy(vt[0:D, :], psum[1][0:D, 0:GROUP]).then_inc(S["vt_ready"], 1)
                        act.wait_ge(S["hid_ready"], g + 1)
                        c = {"w11": B11, "w21": B21, "w31": B31}[wa]
                        nc.scalar.activation(ht[0:hidden, :], psum[2][0:hidden, 0:GROUP], ACT.Relu,
                                             bias=bias[0:hidden, c:c + 1]).then_inc(S["act_ready"], 1)
                        if last:
                            norm_act(act, g)
                            relation_tables_act(act, g, x3)
                        else:
                            act.wait_ge(S["res_ready"], g + 1)
                            nc.scalar.activation(ot, psum[3][:, 0:HD], ACT.Relu).then_inc(S["act2_ready"], 1)
                            act.wait_ge(S["act2_ready"], g + 1)
                            act.dma_start(group_rows(target, g, D), ot).then_inc(S["out_ready"], 16)
                            act.wait_ge(S["out_ready"], 16 * g + 16)
            new_phase()
            gathered_before[0] += LOOPS * 16 * CHUNK

        def relation_tables_pe(pe, g, weights, brow):
            hold(pe, S["xn_ready"], g + 2)
            for h in range(2):
                mm = nc.tensor.transpose(psum[4][0:D, h * P:(h + 1) * P], halves(xn)[:, h, :], ident[:, :])
            mm.then_inc(S["turned"], 1)
            pe.wait_ge(S["xt_ready"], g + 2)
            for h in range(2):
                nc.tensor.matmul(psum[5][:, h * 3 * D:(h + 1) * 3 * D], orow[:, :], brow, start=True, stop=False)
                mm = nc.tensor.matmul(psum[5][:, h * 3 * D:(h + 1) * 3 * D], work[0:D, 2816 + h * P:2816 + (h + 1) * P],
                                      weights, start=False, stop=True)
            mm.then_inc(S["tab_ready"], 1)

        def relation_tables_act(act, g, keep, to=(None, None)):
            rel, own = to if to[0] is not None else (rel_a, self_a)
            act.wait_ge(S["turned"], g + 1)
            nc.scalar.copy(work[0:D, 2816:2816 + GROUP], psum[4][0:D, 0:GROUP]).then_inc(S["xt_ready"], 1)
            act.wait_ge(S["tab_ready"], g + 1)
            nc.scalar.copy(halves(sb_), halves(psum[5][:, 0:6 * D])[:, :, 2 * D:3 * D]).then_inc(S["tab_copied"], 1)
            nc.scalar.copy(halves(hb), halves(psum[5][:, 0:6 * D])[:, :, 0:2 * D]).then_inc(S["tab_copied2"], 1)
            n = 2
            if keep is not None:
                act.dma_start(group_rows(keep, g, D), xn).then_inc(S["out_ready"], 16)
                n = 3
            act.wait_ge(S["tab_copied"], g + 1)
            act.dma_start(group_rows(own, g, D), sb_).then_inc(S["out_ready"], 16)
            act.wait_ge(S["tab_copied2"], g + 1)
            act.dma_start(group_rows(rel, g, HD), hb).then_inc(S["out_ready"], 16)
            act.wait_ge(S["out_ready"], 16 * n * g + 16 * n)
            act.sem_inc(S["stored"], 1)

        gin(x2, gin_a, "w11", "w12", D, B11, "b12", False)
        gin(gin_a, gin_b, "w21", "w22", P, B21, "b22", False)
        gin(gin_b, None, "w31", "w32", D, B31, "b32", True)

        def relational(table, own, weights, brow, to, last):
            with nc.Block() as block:
                @block.gpsimd
                def _(pool):
                    gathers(table.rearrange("n (r d) -> (n r) d", r=2), D, rel_u)

                @block.sync
                def _(sp):
                    place_messages(sp)

                @block.tensor
                def _(pe):
                    pe.sem_inc(S["sel_free"], 2)

                    def node(g):
                        if not last:
                            relation_tables_pe(pe, g, weights, brow)
                    groups(pe, lambda g: reduce_pe(pe, g, D, D, True), nothing, node)

                @block.vector
                def _(dve):
                    from_one(dve, "agg_taken", "xn_ready")
                    v = nc.vector

                    def take(g):
                        dve.wait_ge(S["node_in"], (32 if last else 16) * (g + 1))
                        dve.wait_ge(S["agg_ready"], g + 1)
                        v.tensor_tensor(vs, AGG[:, 0:HD], nin[:, 0:HD], ALU.add).then_inc(S["vsum"], 1)
                        dve.wait_ge(S["vsum"], g + 1)
                        dve.sem_inc(S["agg_taken"], 1)

                    def node(g):
                        dve.wait_ge(S["stored"], g + 1)
                        if last:
                            v.tensor_tensor(ot, vs, nin[:, HD:2 * HD], ALU.add).then_inc(S["evac"], 1)
                            dve.wait_ge(S["evac"], g + 1)
                            norm_dve(dve, g, ot, xn)
                            dve.sem_inc(S["xn_ready"], 1)
                        else:
                            v.tensor_scalar(xn, vs, 0.0, None, ALU.max).then_inc(S["xn_ready"], 1)
                    groups(dve, lambda g: select_dve(dve, g, None), take, node)

                @block.scalar
                def _(act):
                    from_one(act, "stored", "xt_ready")
                    with act.Fori(0, NG) as g:
                        act.dma_start(nin[:, 0:HD], group_rows(own, g, D)).then_inc(S["node_in"], 16)
                        if last:
                            act.dma_start(nin[:, HD:2 * HD], group_rows(x3, g, D)).then_inc(S["node_in"], 16)
                            norm_act(act, g)
                            act.wait_ge(S["xn_ready"], g + 2)
                            act.dma_start(group_rows(out, g, D), xn).then_inc(S["out_ready"], 16)
                            act.wait_ge(S["out_ready"], 16 * g + 16)
                            act.sem_inc(S["stored"], 1)
                        else:
                            relation_tables_act(act, g, None, to)
            new_phase()
            gathered_before[0] += LOOPS * 16 * CHUNK

        relational(rel_a, self_a, w("R1", D), row("rb1"), (rel_b, self_b), False)
        relational(rel_b, self_b, R2[:, :], rb2[:, :], (rel_a, self_a), False)
        relational(rel_a, self_a, None, None, None, True)


def kernel(**inputs):
    import numpy as np
    import concourse.bacc as bacc
    from concourse.bass_utils import run_bass_kernel_spmd

    i = {k: np.asarray(v) for k, v in inputs.items()}
    n, d = i["x"].shape
    e = i["src"].shape[0]
    T, NG = sizes(n, e)
    EP, NP = T * P, NG * GROUP

    def tiles(v, fill=0):
        return np.ascontiguousarray(np.pad(v, (0, EP - e), constant_values=fill).reshape(T, P).T)

    dst = np.pad(i["dst"], (0, EP - e), constant_values=NP)
    prev = np.concatenate([np.full(1, -1, dst.dtype), dst[:-1]])
    nxt = np.concatenate([dst[1:], np.full(1, -1, dst.dtype)])
    Q = T // 4
    ends = np.concatenate([dst[0::P].reshape(4, Q).T, dst[P - 1::P].reshape(4, Q).T], axis=1)
    x_rows = np.pad(i["x"], ((0, NP - n), (0, 0)))
    gs = np.pad(i["edge_attr_64"], ((0, EP - e), (0, 0)))
    col = lambda v: np.ascontiguousarray(v.reshape(-1, 1))
    rw = lambda v: np.ascontiguousarray(v.reshape(1, -1))
    arrays = {
        "src_tiles": tiles(i["src"]), "dst_tiles": np.ascontiguousarray(dst.reshape(T, P).T),
        "next_tiles": np.ascontiguousarray(nxt.reshape(T, P).T), "type_tiles": tiles(i["edge_type_2"]),
        "ew_tiles": tiles(i["edge_weight"]), "dst_flat": dst.reshape(P, T), "prev_flat": prev.reshape(P, T),
        "next_flat": nxt.reshape(P, T), "tile_ends": np.ascontiguousarray(ends),
        "x_rows": x_rows, "x_cols": np.ascontiguousarray(x_rows.T), "gs_cols": np.ascontiguousarray(gs.T),
        "identity": np.eye(P, dtype=np.float32),
        "group_base": np.tile(np.arange(NG, dtype=np.float32) * GROUP, (P, 1)),
        "lane": np.tile((2 * np.arange(P)[None, :] + np.arange(2)[:, None]).reshape(1, -1).astype(np.float32), (P, 1)),
        "fc_w": i["L0_gnn_fc_w"], "attn_l": rw(i["L0_gnn_attn_l"])[0], "attn_r": rw(i["L0_gnn_attn_r"])[0],
        "filt_w1": i["L0_gnn_filt_w1"], "filt_b1": col(i["L0_gnn_filt_b1"]), "filt_w2": i["L0_gnn_filt_w2"],
        "filt_b2": rw(i["L0_gnn_filt_b2"]), "mlp_w1": i["L0_gnn_mlp_w1"], "mlp_b1": col(i["L0_gnn_mlp_b1"]),
        "mlp_w2": i["L0_gnn_mlp_w2"], "mlp_b2": rw(i["L0_gnn_mlp_b2"]), "L1_W": i["L1_gnn_W"], "L1_b": rw(i["L1_gnn_b"]),
    }
    for k in ("11", "12", "21", "22", "31", "32"):
        arrays[f"w{k}"] = i[f"L2_gnn_w{k}"]
        arrays[f"b{k}"] = (col if k[1] == "1" else rw)(i[f"L2_gnn_b{k}"])
    for k in range(3):
        W = i[f"L3_gnn_W{k}"]
        arrays[f"R{k}"] = np.ascontiguousarray(np.concatenate([W[0], W[1], i[f"L3_gnn_Ws{k}"]], axis=1))
        arrays[f"b{k}"] = rw(i[f"L3_gnn_b{k}"])

    nc = bacc.Bacc("TRN2", target_bir_lowering=False, num_devices=1)
    aps = {k: nc.dram_tensor(f"in_{k}", v.shape, mybir.dt.from_np(v.dtype), kind="ExternalInput").ap()
           for k, v in arrays.items()}
    out = nc.dram_tensor("out_rows", (NP, d), F32, kind="ExternalOutput").ap()
    build(nc, aps, out)
    r = run_bass_kernel_spmd(nc, [{f"in_{k}": v for k, v in arrays.items()}], core_ids=[0])
    return r.results[0]["out_rows"][:n]
```
